# Optimizing a Trainium2 kernel written in Bass

```python
import numpy as np
import jax
import jax.numpy as jnp

def _softmax(x, axis=-1):
    return jax.nn.softmax(x, axis=axis)

def _gelu(x):
    return jax.nn.gelu(x, approximate=True)

def _silu(x):
    return jax.nn.silu(x)

def _sigmoid(x):
    return jax.nn.sigmoid(x)

def _layernorm(x, axis=-1, eps=1e-05):
    m = jnp.mean(x, axis=axis, keepdims=True)
    v = jnp.var(x, axis=axis, keepdims=True)
    return (x - m) / jnp.sqrt(v + eps)

def _scatter_add(tgt, idx, src, axis=0):
    return tgt.at[idx].add(src)

def _segment_sum(src, seg, n):
    return jax.ops.segment_sum(src, seg, n)
kernel_name = 'mk_dlrm_tower_d1_rec_r8_4579c4'

def setup_inputs(seed: int=0):
    np.random.seed(seed)
    _w = jnp.asarray

    def _rec_inputs():
        import jax
        import jax.numpy as jnp
        _tk = jax.random.key(seed)
        dense_ctx = jax.random.normal(jax.random.fold_in(_tk, 190), (512, 16), jnp.float32)
        ids = jnp.stack([jax.random.randint(jax.random.fold_in(_tk, 200 + f), (512,), 0, v, jnp.int32) for f, v in enumerate([12500, 1250, 1000, 12500, 1250, 1000, 12500, 1250, 1250, 1000, 1250, 1250, 1250, 1000, 1000, 1250, 1250, 12500, 12500, 12500, 1000, 1000, 1000, 1250, 1000, 1250, 1000, 1250, 1250, 1000, 1250, 1000])], axis=1)
        tbl_0 = 0.05 * jax.random.normal(jax.random.fold_in(_tk, 500 + 0), (12500, 256), jnp.float32)
        tbl_1 = 0.05 * jax.random.normal(jax.random.fold_in(_tk, 500 + 1), (1250, 256), jnp.float32)
        tbl_2 = 0.05 * jax.random.normal(jax.random.fold_in(_tk, 500 + 2), (1000, 256), jnp.float32)
        tbl_3 = 0.05 * jax.random.normal(jax.random.fold_in(_tk, 500 + 3), (12500, 256), jnp.float32)
        tbl_4 = 0.05 * jax.random.normal(jax.random.fold_in(_tk, 500 + 4), (1250, 256), jnp.float32)
        tbl_5 = 0.05 * jax.random.normal(jax.random.fold_in(_tk, 500 + 5), (1000, 256), jnp.float32)
        tbl_6 = 0.05 * jax.random.normal(jax.random.fold_in(_tk, 500 + 6), (12500, 256), jnp.float32)
        tbl_7 = 0.05 * jax.random.normal(jax.random.fold_in(_tk, 500 + 7), (1250, 256), jnp.float32)
        tbl_8 = 0.05 * jax.random.normal(jax.random.fold_in(_tk, 500 + 8), (1250, 256), jnp.float32)
        tbl_9 = 0.05 * jax.random.normal(jax.random.fold_in(_tk, 500 + 9), (1000, 256), jnp.float32)
        tbl_10 = 0.05 * jax.random.normal(jax.random.fold_in(_tk, 500 + 10), (1250, 256), jnp.float32)
        tbl_11 = 0.05 * jax.random.normal(jax.random.fold_in(_tk, 500 + 11), (1250, 256), jnp.float32)
        tbl_12 = 0.05 * jax.random.normal(jax.random.fold_in(_tk, 500 + 12), (1250, 256), jnp.float32)
        tbl_13 = 0.05 * jax.random.normal(jax.random.fold_in(_tk, 500 + 13), (1000, 256), jnp.float32)
        tbl_14 = 0.05 * jax.random.normal(jax.random.fold_in(_tk, 500 + 14), (1000, 256), jnp.float32)
        tbl_15 = 0.05 * jax.random.normal(jax.random.fold_in(_tk, 500 + 15), (1250, 256), jnp.float32)
        tbl_16 = 0.05 * jax.random.normal(jax.random.fold_in(_tk, 500 + 16), (1250, 256), jnp.float32)
        tbl_17 = 0.05 * jax.random.normal(jax.random.fold_in(_tk, 500 + 17), (12500, 256), jnp.float32)
        tbl_18 = 0.05 * jax.random.normal(jax.random.fold_in(_tk, 500 + 18), (12500, 256), jnp.float32)
        tbl_19 = 0.05 * jax.random.normal(jax.random.fold_in(_tk, 500 + 19), (12500, 256), jnp.float32)
        tbl_20 = 0.05 * jax.random.normal(jax.random.fold_in(_tk, 500 + 20), (1000, 256), jnp.float32)
        tbl_21 = 0.05 * jax.random.normal(jax.random.fold_in(_tk, 500 + 21), (1000, 256), jnp.float32)
        tbl_22 = 0.05 * jax.random.normal(jax.random.fold_in(_tk, 500 + 22), (1000, 256), jnp.float32)
        tbl_23 = 0.05 * jax.random.normal(jax.random.fold_in(_tk, 500 + 23), (1250, 256), jnp.float32)
        tbl_24 = 0.05 * jax.random.normal(jax.random.fold_in(_tk, 500 + 24), (1000, 256), jnp.float32)
        tbl_25 = 0.05 * jax.random.normal(jax.random.fold_in(_tk, 500 + 25), (1250, 256), jnp.float32)
        tbl_26 = 0.05 * jax.random.normal(jax.random.fold_in(_tk, 500 + 26), (1000, 256), jnp.float32)
        tbl_27 = 0.05 * jax.random.normal(jax.random.fold_in(_tk, 500 + 27), (1250, 256), jnp.float32)
        tbl_28 = 0.05 * jax.random.normal(jax.random.fold_in(_tk, 500 + 28), (1250, 256), jnp.float32)
        tbl_29 = 0.05 * jax.random.normal(jax.random.fold_in(_tk, 500 + 29), (1000, 256), jnp.float32)
        tbl_30 = 0.05 * jax.random.normal(jax.random.fold_in(_tk, 500 + 30), (1250, 256), jnp.float32)
        tbl_31 = 0.05 * jax.random.normal(jax.random.fold_in(_tk, 500 + 31), (1000, 256), jnp.float32)
        _rk = jax.random.fold_in(_tk, 7)
        W_top1 = 0.0441942 * jax.random.normal(jax.random.fold_in(_tk, 801), (512, 512), jnp.float32)
        W_top2 = 0.0441942 * jax.random.normal(jax.random.fold_in(_tk, 802), (512, 256), jnp.float32)
        W_top3 = 0.0625 * jax.random.normal(jax.random.fold_in(_tk, 803), (256, 1), jnp.float32)
        b_top1 = jnp.zeros((512,), jnp.float32)
        b_top2 = jnp.zeros((256,), jnp.float32)
        return (dense_ctx, ids, tbl_0, tbl_1, tbl_2, tbl_3, tbl_4, tbl_5, tbl_6, tbl_7, tbl_8, tbl_9, tbl_10, tbl_11, tbl_12, tbl_13, tbl_14, tbl_15, tbl_16, tbl_17, tbl_18, tbl_19, tbl_20, tbl_21, tbl_22, tbl_23, tbl_24, tbl_25, tbl_26, tbl_27, tbl_28, tbl_29, tbl_30, tbl_31, W_top1, b_top1, W_top2, b_top2, W_top3)
    dense_ctx, ids, tbl_0, tbl_1, tbl_2, tbl_3, tbl_4, tbl_5, tbl_6, tbl_7, tbl_8, tbl_9, tbl_10, tbl_11, tbl_12, tbl_13, tbl_14, tbl_15, tbl_16, tbl_17, tbl_18, tbl_19, tbl_20, tbl_21, tbl_22, tbl_23, tbl_24, tbl_25, tbl_26, tbl_27, tbl_28, tbl_29, tbl_30, tbl_31, W_top1, b_top1, W_top2, b_top2, W_top3 = _rec_inputs()

    def _L0_rec_setup():
        import jax, jax.numpy as jnp
        import numpy as np
        B, N, D = (1024, 32, 256)
        key = jax.random.key(seed)
        x = jax.random.normal(key, (B, N, D), dtype=jnp.float32)
        return {'x': x}
    _L0_rec_all = _L0_rec_setup()
    _L0_rec_in = {k: v for k, v in _L0_rec_all.items() if k in ()}
    del _L0_rec_all
    return {'dense_ctx': dense_ctx, 'ids': ids, 'tbl_0': tbl_0, 'tbl_1': tbl_1, 'tbl_2': tbl_2, 'tbl_3': tbl_3, 'tbl_4': tbl_4, 'tbl_5': tbl_5, 'tbl_6': tbl_6, 'tbl_7': tbl_7, 'tbl_8': tbl_8, 'tbl_9': tbl_9, 'tbl_10': tbl_10, 'tbl_11': tbl_11, 'tbl_12': tbl_12, 'tbl_13': tbl_13, 'tbl_14': tbl_14, 'tbl_15': tbl_15, 'tbl_16': tbl_16, 'tbl_17': tbl_17, 'tbl_18': tbl_18, 'tbl_19': tbl_19, 'tbl_20': tbl_20, 'tbl_21': tbl_21, 'tbl_22': tbl_22, 'tbl_23': tbl_23, 'tbl_24': tbl_24, 'tbl_25': tbl_25, 'tbl_26': tbl_26, 'tbl_27': tbl_27, 'tbl_28': tbl_28, 'tbl_29': tbl_29, 'tbl_30': tbl_30, 'tbl_31': tbl_31, 'W_top1': W_top1, 'b_top1': b_top1, 'W_top2': W_top2, 'b_top2': b_top2, 'W_top3': W_top3}

def reference(dense_ctx, ids, tbl_0, tbl_1, tbl_2, tbl_3, tbl_4, tbl_5, tbl_6, tbl_7, tbl_8, tbl_9, tbl_10, tbl_11, tbl_12, tbl_13, tbl_14, tbl_15, tbl_16, tbl_17, tbl_18, tbl_19, tbl_20, tbl_21, tbl_22, tbl_23, tbl_24, tbl_25, tbl_26, tbl_27, tbl_28, tbl_29, tbl_30, tbl_31, W_top1, b_top1, W_top2, b_top2, W_top3):
    import jax
    import jax.numpy as jnp

    def _L0_rec_ref(x):
        import jax, jax.numpy as jnp
        import numpy as np
        B, N, D = (1024, 32, 256)
        'Second-order feature interaction (DLRM dot interaction).\n\n            Computes dot(x_i, x_j) for all field pairs i < j (self_interaction=False),\n            flattened in row-major upper-triangular order -> [B, N*(N-1)/2].\n            Matches tf.boolean_mask(dot_products, strictly_upper_mask) ordering.\n            '
        b, n, d = x.shape
        iu, ju = jnp.triu_indices(n, k=1)
        dots = jnp.einsum('bnd,bmd->bnm', x, x)
        return dots[:, iu, ju]
    e = jnp.stack([tbl_0[ids[:, 0]], tbl_1[ids[:, 1]], tbl_2[ids[:, 2]], tbl_3[ids[:, 3]], tbl_4[ids[:, 4]], tbl_5[ids[:, 5]], tbl_6[ids[:, 6]], tbl_7[ids[:, 7]], tbl_8[ids[:, 8]], tbl_9[ids[:, 9]], tbl_10[ids[:, 10]], tbl_11[ids[:, 11]], tbl_12[ids[:, 12]], tbl_13[ids[:, 13]], tbl_14[ids[:, 14]], tbl_15[ids[:, 15]], tbl_16[ids[:, 16]], tbl_17[ids[:, 17]], tbl_18[ids[:, 18]], tbl_19[ids[:, 19]], tbl_20[ids[:, 20]], tbl_21[ids[:, 21]], tbl_22[ids[:, 22]], tbl_23[ids[:, 23]], tbl_24[ids[:, 24]], tbl_25[ids[:, 25]], tbl_26[ids[:, 26]], tbl_27[ids[:, 27]], tbl_28[ids[:, 28]], tbl_29[ids[:, 29]], tbl_30[ids[:, 30]], tbl_31[ids[:, 31]]], axis=1)
    z = _L0_rec_ref(e)
    z = z.reshape(z.shape[0], -1)
    h = jnp.concatenate([z, dense_ctx], axis=1)
    h = jnp.maximum(h @ W_top1 + b_top1, 0.0)
    h = jnp.maximum(h @ W_top2 + b_top2, 0.0)
    y = h @ W_top3
    return y

_drawn_inputs = setup_inputs


def setup_inputs(seed=0):
    import zlib

    import numpy as np

    out = dict(_drawn_inputs(seed))
    spreads = {'b_top1': (0.0, 0.1), 'b_top2': (0.0, 0.1)}
    factors = {}
    for name, (base, spread) in spreads.items():
        noise = np.random.default_rng([zlib.crc32(name.encode()), seed]).standard_normal(out[name].shape)
        drawn = base * np.exp(spread * noise) if base else spread * noise
        out[name] = jnp.asarray(drawn.astype(out[name].dtype))
    for name, factor in factors.items():
        out[name] = (out[name] * factor).astype(out[name].dtype)
    return out
```

```python
import concourse.bass as bass
from concourse import mybir
from contextlib import ExitStack

FIELDS = 32
DIM = 256
BATCH = 512
CONTEXT = 16
HIDDEN1 = 512
HIDDEN2 = 256
P = 128

LANES = P // FIELDS
HALVES = DIM // P
BLOCK = P
GROUPS = BLOCK // LANES
BLOCKS = BATCH // BLOCK
PAIR = 2
PAIRS = GROUPS // PAIR
OCTET = 8
OCTETS = GROUPS // OCTET
COLS = FIELDS // 4
N1 = HIDDEN1 // P
N2 = HIDDEN2 // P
TURNED_BUFS = 4
REFILL = GROUPS // 2


def dlrm_tower(nc, ids, tables, context_t, w1, b1, w2, b2, w3, out):
    fp32 = mybir.dt.float32
    int32 = mybir.dt.int32
    ALU = mybir.AluOpType
    ACT = mybir.ActivationFunctionType

    ctx = ExitStack()
    with ctx:
        def sb(name, shape, dt=fp32):
            return ctx.enter_context(nc.sbuf_tensor(name, shape, dt))

        def ps(name, shape):
            return ctx.enter_context(nc.psum_tensor(name, shape, fp32))

        def sem(name):
            return ctx.enter_context(nc.semaphore(name))

        ids_sb = sb("ids_sb", [P, 1 + BLOCKS * GROUPS], int32)
        rows_now = [sb(f"rows_now{half}", [P, REFILL], int32) for half in range(2)]
        ident = sb("ident", [P, P])
        emb = sb("emb", [P, GROUPS, DIM])
        turned = sb("turned", [P, TURNED_BUFS, PAIR, HALVES, P])
        z = sb("z", [P, COLS, LANES, GROUPS])
        w1_sb = sb("w1_sb", [P, COLS, HIDDEN1])
        w2_sb = sb("w2_sb", [P, N1, HIDDEN2])
        w3_sb = sb("w3_sb", [P, N2])
        b1_sb = sb("b1_sb", [P, N1])
        b2_sb = sb("b2_sb", [P, N2])
        context_sb = sb("context_sb", [CONTEXT, BATCH])
        h1 = sb("h1", [P, N1, BLOCK])
        h2 = sb("h2", [P, N2, BLOCK])
        y = sb("y", [1, BATCH])

        turned_ps = [ps("turned_ps0", [P, PAIR, HALVES, P]), ps("turned_ps1", [P, PAIR, HALVES, P])]
        dots_ps = [ps("dots_ps0", [P, OCTET, P]), ps("dots_ps1", [P, OCTET, P])]
        tail_ps = [ps(f"tail_ps{m}", [P, 512]) for m in range(N2)]
        h1_ps = [dots_ps[n // 2][:, (n % 2) * (OCTET // 2), :] for n in range(N1)]
        h2_ps = [tail_ps[m][:, 0:BLOCK] for m in range(N2)]
        y_ps = tail_ps[0][0:1, BLOCK:2 * BLOCK]

        ids_in = sem("ids_in")
        refilled = [sem("refilled0"), sem("refilled1")]
        ident_zero = sem("ident_zero")
        ident_set = sem("ident_set")
        gathered = [sem(f"gathered{s}") for s in range(GROUPS)]
        weights_in = sem("weights_in")
        w2_in = sem("w2_in")
        w3_in = sem("w3_in")
        b1_in = sem("b1_in")
        b2_in = sem("b2_in")
        context_in = sem("context_in")
        transposed = sem("transposed")
        copied_dve = sem("copied_dve")
        copied_act = sem("copied_act")
        dotted_pair = sem("dotted_pair")
        dotted = sem("dotted")
        z_dve = sem("z_dve")
        z_act = sem("z_act")
        z_context = sem("z_context")
        z_zero = sem("z_zero")
        h1_done = sem("h1_done")
        h1_relu = sem("h1_relu")
        h2_done = sem("h2_done")
        h2_relu = sem("h2_relu")
        y_done = sem("y_done")
        y_copied = sem("y_copied")
        stored = sem("stored")

        block = ctx.enter_context(nc.Block())

        @block.sync
        def _(sp):
            sp.dma_start(ids_sb[:, :], ids).then_inc(ids_in, 16)
            sp.dma_start(w1_sb[:, :, :], w1).then_inc(weights_in, 16)
            sp.dma_start(context_sb[:, :], context_t).then_inc(context_in, 16)
            sp.dma_start(w2_sb[:, :, :], w2.rearrange("(k p) m -> p k m", p=P)).then_inc(w2_in, 16)
            sp.dma_start(b1_sb[:, :], b1).then_inc(b1_in, 16)
            sp.dma_start(b2_sb[:, :], b2).then_inc(b2_in, 16)
            sp.dma_start(w3_sb[:, :], w3).then_inc(w3_in, 16)
            sp.wait_ge(y_copied, BLOCKS)
            sp.dma_start(out, y[:, :]).then_inc(stored, 16)
            sp.wait_ge(stored, 16)

        @block.gpsimd
        def _(pool):
            def gather(s):
                pool.indirect_dma_start(
                    emb[:, s, :], None, tables,
                    bass.IndirectOffsetOnAxis(ap=rows_now[s // REFILL][:, s % REFILL:s % REFILL + 1], axis=0),
                ).then_inc(gathered[s], 16)

            pool.memset(ident[:, :], 0.0).then_inc(ident_zero, 1)
            pool.wait_ge(ident_zero, 1)
            pool.affine_select(out=ident[:, :], in_=ident[:, :], compare_op=ALU.not_equal, fill=1.0,
                               base=0, pattern=[[-1, P]], channel_multiplier=1).then_inc(ident_set, 1)
            for s in range(GROUPS):
                if s % REFILL == 0:
                    pool.wait_ge(refilled[s // REFILL], 1)
                gather(s)
            with pool.Fori(1, BLOCKS) as t:
                for s in range(GROUPS):
                    if s % REFILL == 0:
                        pool.wait_ge(refilled[s // REFILL], t + 1)
                    if s % PAIR == 0:
                        pool.wait_ge(transposed, PAIRS * t + (s // PAIR + 1 - PAIRS))
                    if s % PAIR == 0:
                        pool.nop(nofuse=True)
                    gather(s)

        @block.tensor
        def _(pe):
            def transposes(k, t):
                for g in range(PAIR):
                    pe.wait_ge(gathered[PAIR * k + g], 16 * t + 16)
                    if g == 0 and k >= 2:
                        pe.wait_ge(copied_act if k % 2 else copied_dve, (PAIRS // 2) * t + (k // 2))
                    for h in range(HALVES):
                        last = nc.tensor.transpose(turned_ps[k % 2][:, g, h, :],
                                                   emb[:, PAIR * k + g, h * P:(h + 1) * P], ident[:, :])
                last.then_inc(transposed, 1)

            def dots(k, t):
                q, first = divmod(PAIR * k, OCTET)
                pe.wait_ge(copied_act if k % 2 else copied_dve, (PAIRS // 2) * t + (k // 2 + 1))
                if first == 0 and q >= 2:
                    pe.wait_ge(z_dve, OCTETS * t + (q - 1))
                    pe.wait_ge(z_act, OCTETS * t + (q - 1))
                for g in range(PAIR):
                    for h in range(HALVES):
                        part = turned[:, k % TURNED_BUFS, g, h, :]
                        last = nc.tensor.matmul(dots_ps[q % 2][:, first + g, :], part, part,
                                                start=(h == 0), stop=(h == HALVES - 1))
                last.then_inc(dotted_pair, 1)

            def layers(t):
                pe.wait_ge(z_dve, OCTETS * t + OCTETS)
                pe.wait_ge(z_act, OCTETS * t + OCTETS)
                pe.wait_ge(z_context, t + 1)
                for n in range(N1):
                    for j in range(COLS):
                        last = nc.tensor.matmul(h1_ps[n], w1_sb[:, j, n * P:(n + 1) * P],
                                                z[:, j, :, :].rearrange("p l g -> p (l g)"),
                                                start=(j == 0), stop=(j == COLS - 1))
                    last.then_inc(h1_done, 1)
                pe.wait_ge(h1_relu, N1 * t + N1)
                for m in range(N2):
                    for n in range(N1):
                        last = nc.tensor.matmul(h2_ps[m], w2_sb[:, n, m * P:(m + 1) * P], h1[:, n, :],
                                                start=(n == 0), stop=(n == N1 - 1))
                    last.then_inc(h2_done, 1)
                pe.wait_ge(h2_relu, N2 * t + N2)
                for m in range(N2):
                    last = nc.tensor.matmul(y_ps, w3_sb[:, m:m + 1], h2[:, m, :],
                                            start=(m == 0), stop=(m == N2 - 1))
                last.then_inc(y_done, 1)

            pe.wait_ge(ident_set, 1)
            pe.wait_ge(weights_in, 16)
            pe.wait_ge(w2_in, 16)
            pe.wait_ge(w3_in, 16)
            with pe.Fori(0, BLOCKS) as t:
                for k in range(PAIRS):
                    transposes(k, t)
                    if k:
                        dots(k - 1, t)
                dots(PAIRS - 1, t)
                layers(t)

        def samples(t):
            return slice(t * BLOCK, (t + 1) * BLOCK) if isinstance(t, int) else bass.ds(t * BLOCK, BLOCK)

        def spread(copy, q, lanes):
            for lane in lanes:
                for c in range(P // FIELDS):
                    j = 1 if c == 0 else 0
                    at = lane * FIELDS + c * COLS
                    src = dots_ps[q % 2][lane * FIELDS:(lane + 1) * FIELDS, :, at + j:at + COLS]
                    dst = z[c * FIELDS:(c + 1) * FIELDS, j:COLS, lane, q * OCTET:(q + 1) * OCTET]
                    last = copy(dst.rearrange("p j g -> p g j"), src)
            return last

        @block.vector
        def _(dve):
            def refill(half, at):
                nc.vector.tensor_scalar(rows_now[half][:, :], ids_sb[:, at], ids_sb[:, 0:1], None,
                                        ALU.add).then_inc(refilled[half], 1)

            def context_into_z(t):
                nc.vector.tensor_copy(z[0:CONTEXT, 0, :, :].rearrange("p l g -> p (l g)"),
                                      context_sb[:, samples(t)]).then_inc(z_context, 1)

            def block_of(t, last):
                for k in range(PAIRS + 1):
                    if k == PAIRS // 2 + 1 and not last:
                        refill(0, bass.ds(t * GROUPS + (1 + GROUPS), REFILL))
                    if k == PAIRS and not last:
                        dve.wait_ge(transposed, PAIRS * t + PAIRS)
                        refill(1, bass.ds(t * GROUPS + (1 + GROUPS + REFILL), REFILL))
                    if k % 2 == 0 and k < PAIRS:
                        dve.wait_ge(transposed, PAIRS * t + (k + 1))
                        if k >= TURNED_BUFS:
                            dve.wait_ge(dotted_pair, PAIRS * t + (k - TURNED_BUFS + 1))
                        nc.vector.tensor_copy(turned[:, k % TURNED_BUFS, :, :, :], turned_ps[k % 2][:, :, :, :])\
                            .then_inc(copied_dve, 1)
                    if k % (OCTET // PAIR) == 0 and k:
                        q = k // (OCTET // PAIR) - 1
                        dve.wait_ge(dotted_pair, PAIRS * t + (OCTET // PAIR) * (q + 1))
                        spread(nc.vector.tensor_copy, q, (0, 1)).then_inc(z_dve, 1)
                    if k == PAIRS // 2:
                        context_into_z(t)
                for n in range(N1):
                    dve.wait_ge(h1_done, N1 * t + (n + 1))
                    nc.vector.tensor_scalar(h1[:, n, :], h1_ps[n], b1_sb[:, n:n + 1], 0.0,
                                            ALU.add, ALU.max).then_inc(h1_relu, 1)
                for m in range(N2):
                    dve.wait_ge(h2_done, N2 * t + (m + 1))
                    nc.vector.tensor_scalar(h2[:, m, :], h2_ps[m], b2_sb[:, m:m + 1], 0.0,
                                            ALU.add, ALU.max).then_inc(h2_relu, 1)
                dve.wait_ge(y_done, t + 1)
                nc.vector.tensor_copy(y[:, samples(t)], y_ps).then_inc(y_copied, 1)

            dve.wait_ge(ids_in, 16)
            refill(0, slice(1, 1 + REFILL))
            refill(1, slice(1 + REFILL, 1 + GROUPS))
            nc.vector.memset(z[0:FIELDS, 0, :, :], 0.0).then_inc(z_zero, 1)
            dve.wait_ge(z_zero, 1)
            dve.wait_ge(context_in, 16)
            dve.wait_ge(b1_in, 16)
            dve.wait_ge(b2_in, 16)
            with dve.Fori(0, BLOCKS - 1) as t:
                block_of(t, False)
            block_of(BLOCKS - 1, True)

        @block.scalar
        def _(act):
            with act.Fori(0, BLOCKS) as t:
                for k in range(PAIRS + 1):
                    if k % 2:
                        act.wait_ge(transposed, PAIRS * t + (k + 1))
                        if k >= TURNED_BUFS:
                            act.wait_ge(dotted_pair, PAIRS * t + (k - TURNED_BUFS + 1))
                        nc.scalar.copy(turned[:, k % TURNED_BUFS, :, :, :], turned_ps[k % 2][:, :, :, :])\
                            .then_inc(copied_act, 1)
                    if k % (OCTET // PAIR) == 0 and k:
                        q = k // (OCTET // PAIR) - 1
                        act.wait_ge(dotted_pair, PAIRS * t + (OCTET // PAIR) * (q + 1))
                        spread(nc.scalar.copy, q, (2, 3)).then_inc(z_act, 1)


def _pair_rows():
    import numpy as np
    at = -np.ones((P, COLS), np.int64)
    i, j = np.triu_indices(FIELDS, k=1)
    at[(j // COLS) * FIELDS + i, j % COLS] = np.arange(len(i))
    at[np.arange(CONTEXT), 0] = len(i) + np.arange(CONTEXT)
    return at


def kernel(**inputs):
    import numpy as np
    import concourse.bacc as bacc
    from concourse.bass_utils import run_bass_kernel_spmd

    tables = [np.asarray(inputs[f"tbl_{f}"]) for f in range(FIELDS)]
    first_row = np.concatenate([[0], np.cumsum([t.shape[0] for t in tables])[:-1]]).astype(np.int32)
    ids = np.asarray(inputs["ids"]).reshape(BLOCKS, LANES, GROUPS, FIELDS)
    w1 = np.asarray(inputs["W_top1"])
    at = _pair_rows()
    w1_planes = np.zeros((P, COLS, HIDDEN1), w1.dtype)
    w1_planes[at >= 0] = w1[at[at >= 0]]
    arrays = {
        "ids": np.concatenate([np.tile(first_row, LANES).reshape(P, 1),
                               ids.transpose(1, 3, 0, 2).reshape(P, BLOCKS * GROUPS)], axis=1),
        "tables": np.concatenate(tables, axis=0),
        "context_t": np.ascontiguousarray(np.asarray(inputs["dense_ctx"]).T),
        "w1": w1_planes,
        "b1": np.ascontiguousarray(np.asarray(inputs["b_top1"]).reshape(N1, P).T),
        "w2": np.asarray(inputs["W_top2"]),
        "b2": np.ascontiguousarray(np.asarray(inputs["b_top2"]).reshape(N2, P).T),
        "w3": np.ascontiguousarray(np.asarray(inputs["W_top3"]).reshape(N2, P).T),
    }
    nc = bacc.Bacc("TRN2", target_bir_lowering=False, num_devices=1)
    args = [nc.dram_tensor(name, a.shape, mybir.dt.from_np(a.dtype), kind="ExternalInput").ap()
            for name, a in arrays.items()]
    out = nc.dram_tensor("y_out", (1, BATCH), mybir.dt.float32, kind="ExternalOutput").ap()
    dlrm_tower(nc, *args, out)
    r = run_bass_kernel_spmd(nc, [arrays], core_ids=[0])
    return r.results[0]["y_out"].reshape(BATCH, 1)
```

```python
import concourse.bass as bass
from concourse import mybir
from contextlib import ExitStack

FIELDS = 32
DIM = 256
BATCH = 512
CONTEXT = 16
HIDDEN1 = 512
HIDDEN2 = 256
P = 128

LANES = P // FIELDS
HALVES = DIM // P
BLOCK = P
GROUPS = BLOCK // LANES
BLOCKS = BATCH // BLOCK
PAIR = 2
PAIRS = GROUPS // PAIR
QUAD = 4
QUADS = GROUPS // QUAD
PER_QUAD = QUAD // PAIR
OCTET = 8
OCTETS = GROUPS // OCTET
PER_OCTET = OCTET // PAIR
COLS = FIELDS // (P // FIELDS)
N1 = HIDDEN1 // P
N2 = HIDDEN2 // P
SPLIT_BUFS = 4
REFILL = GROUPS // 2
PART = LANES * OCTET
PARTS = P // PART
NARROW = HIDDEN1 // 2
LAG = 2
FIRST_PARTS = PER_OCTET + LAG + 1
W1_LOADS = 4


def dlrm_tower(nc, ids, tables, context_t, w1, w1c, b1, w2, b2, w3, out):
    fp32 = mybir.dt.float32
    int32 = mybir.dt.int32
    ALU = mybir.AluOpType
    ACT = mybir.ActivationFunctionType

    ctx = ExitStack()
    with ctx:
        def sb(name, shape, dt=fp32):
            return ctx.enter_context(nc.sbuf_tensor(name, shape, dt))

        def ps(name, shape):
            return ctx.enter_context(nc.psum_tensor(name, shape, fp32))

        def sem(name):
            return ctx.enter_context(nc.semaphore(name))

        ids_sb = sb("ids_sb", [P, 1 + BLOCKS * GROUPS], int32)
        rows_now = [sb(f"rows_now{half}", [P, REFILL], int32) for half in range(2)]
        ident = sb("ident", [P, P])
        emb = sb("emb", [P, GROUPS, DIM])
        split = sb("split", [P, SPLIT_BUFS, PAIR, HALVES, 2, P], mybir.dt.float32r)
        whole = sb("whole", [P, QUAD, HALVES, P])
        halved = sb("halved", [P, 2, QUAD, FIELDS])
        z = sb("z", [P, COLS, BLOCK])
        w1_sb = sb("w1_sb", [P, COLS, HIDDEN1])
        w1c_sb = sb("w1c_sb", [CONTEXT, HIDDEN1])
        w2_sb = sb("w2_sb", [P, N1, HIDDEN2])
        w3_sb = sb("w3_sb", [P, N2])
        b1_sb = sb("b1_sb", [P, N1])
        b2_sb = sb("b2_sb", [P, N2])
        context_sb = sb("context_sb", [CONTEXT, BATCH])
        context_now = sb("context_now", [CONTEXT, BLOCK])
        fold = sb("fold", [P, PART])
        parts = [sb(f"parts{i}", [P, 2, NARROW]) for i in range(2)]
        h1 = sb("h1", [P, N1, BLOCK])
        h2 = sb("h2", [P, N2, BLOCK])
        y = sb("y", [1, BATCH])

        turned_ps = [ps("turned_ps0", [P, PAIR, HALVES, P]), ps("turned_ps1", [P, PAIR, HALVES, P])]
        dots_ps = [ps(f"dots_ps{i}", [P, QUAD, 2, P]) for i in range(2)]
        tail_ps = [ps(f"tail_ps{i}", [P, 512]) for i in range(2)]
        parts_ps = [tail_ps[i][:, 0:NARROW] for i in range(2)]
        folded_ps = [tail_ps[n // 2][:, NARROW + (n % 2) * PART:NARROW + (n % 2 + 1) * PART] for n in range(N1)]
        h2_ps = [tail_ps[m][:, 0:BLOCK] for m in range(N2)]
        y_ps = tail_ps[1][0:1, BLOCK:2 * BLOCK]
        late_folded_ps = [dots_ps[0][:, n, 0, 0:PART] for n in range(N1)]
        late_y_ps = dots_ps[0][0:1, 0, 0, :]
        late_h2_ps = [dots_ps[1][:, m * QUAD // N2, 0, :] for m in range(N2)]

        ids_in = sem("ids_in")
        refilled = [sem("refilled0"), sem("refilled1")]
        ident_zero = sem("ident_zero")
        ident_set = sem("ident_set")
        gathered = [sem(f"gathered{s}") for s in range(GROUPS)]
        w1_in = sem("w1_in")
        w1c_in = sem("w1c_in")
        w2_in = sem("w2_in")
        w3_in = sem("w3_in")
        b1_in = sem("b1_in")
        b2_in = sem("b2_in")
        context_in = sem("context_in")
        context_set = sem("context_set")
        transposed = sem("transposed")
        rounded = sem("rounded")
        rest_set = sem("rest_set")
        dotted = sem("dotted")
        halved_set = sem("halved_set")
        z_set = sem("z_set")
        z_act = sem("z_act")
        whole_set = sem("whole_set")
        h2_done = sem("h2_done")
        h2_dve = sem("h2_dve")
        h2_act = sem("h2_act")
        y_done = sem("y_done")
        fold_set = sem("fold_set")
        parts_done = sem("parts_done")
        parts_set = [sem(f"parts_set{i}") for i in range(2)]
        folded = [sem(f"folded{i}") for i in range(2)]
        h1_set = [sem(f"h1_set{i}") for i in range(2)]
        y_copied = sem("y_copied")
        stored = sem("stored")

        block = ctx.enter_context(nc.Block())

        @block.sync
        def _(sp):
            sp.dma_start(ids_sb[:, :], ids).then_inc(ids_in, 16)
            sp.dma_start(b1_sb[:, :], b1).then_inc(b1_in, 16)
            sp.dma_start(b2_sb[:, :], b2).then_inc(b2_in, 16)
            sp.dma_start(w3_sb[:, :], w3).then_inc(w3_in, 16)
            sp.dma_start(context_sb[:, :], context_t).then_inc(context_in, 16)
            sp.dma_start(w1c_sb[:, :], w1c).then_inc(w1c_in, 16)
            for i in range(W1_LOADS):
                sp.wait_ge(gathered[PAIR * (i + 1)], 16)
                planes = slice(i * COLS // W1_LOADS, (i + 1) * COLS // W1_LOADS)
                sp.dma_start(w1_sb[:, planes, :], w1[:, planes, :]).then_inc(w1_in, 16)
            sp.wait_ge(gathered[PAIR * (W1_LOADS + 1)], 16)
            sp.dma_start(w2_sb[:, :, :], w2.rearrange("(k p) m -> p k m", p=P)).then_inc(w2_in, 16)
            sp.wait_ge(y_copied, BLOCKS)
            sp.dma_start(out, y[:, :]).then_inc(stored, 16)
            sp.wait_ge(stored, 16)

        @block.gpsimd
        def _(pool):
            def gather(s):
                pool.indirect_dma_start(
                    emb[:, s, :], None, tables,
                    bass.IndirectOffsetOnAxis(ap=rows_now[s // REFILL][:, s % REFILL:s % REFILL + 1], axis=0),
                ).then_inc(gathered[s], 16)

            pool.memset(ident[:, :], 0.0).then_inc(ident_zero, 1)
            pool.wait_ge(ident_zero, 1)
            pool.affine_select(out=ident[:, :], in_=ident[:, :], compare_op=ALU.not_equal, fill=1.0,
                               base=0, pattern=[[-1, P]], channel_multiplier=1).then_inc(ident_set, 1)
            for s in range(GROUPS):
                if s % REFILL == 0:
                    pool.wait_ge(refilled[s // REFILL], 1)
                gather(s)
            with pool.Fori(1, BLOCKS) as t:
                for s in range(GROUPS):
                    if s % REFILL == 0:
                        pool.wait_ge(refilled[s // REFILL], t + 1)
                    if s % PAIR == 0:
                        pool.wait_ge(transposed, PAIRS * t + (s // PAIR + 1 - PAIRS))
                    if s % PAIR == 0:
                        pool.nop(nofuse=True)
                    gather(s)

        LAYER2 = FIRST_PARTS - 1
        OUTPUT = LAYER2 + PER_OCTET

        CATCH_UP = PAIRS - 5

        def dots_due(k, last):
            if last and k >= CATCH_UP:
                return [k - LAG, k - 1] if k == CATCH_UP else [k - 1]
            return [k - LAG]

        def spread_due(k, last):
            if last and k >= CATCH_UP - LAG:
                return {CATCH_UP - 2: 3, CATCH_UP: 4, CATCH_UP + 1: 5}.get(k), range(LANES)
            q, second = divmod(k - PER_QUAD - LAG + 1, PER_QUAD)
            if q % PER_QUAD:
                return (None if second else q), range(LANES)
            return q, range(second * LANES // 2, (second + 1) * LANES // 2)

        def octet_due(k, offset):
            q, rest = divmod(k - FIRST_PARTS - offset, PER_OCTET)
            return (None, None) if rest else (q % OCTETS, 1 if q < 0 else 0)

        def due(k, offset, first, last):
            q, back = octet_due(k, offset)
            if q is None or (first and back) or (last and not back and q >= 2):
                return []
            return [(q, back)]

        def samples(t):
            return slice(t * BLOCK, (t + 1) * BLOCK) if isinstance(t, int) else bass.ds(t * BLOCK, BLOCK)

        def spread_whole(halve, lanes):
            octet, place = divmod((QUADS - 1) * QUAD, OCTET)
            for lane in lanes:
                at_z = octet * PART + lane * OCTET + place
                for c in range(P // FIELDS):
                    at = lane * FIELDS + c * COLS
                    dst = z[c * FIELDS:(c + 1) * FIELDS, :, at_z:at_z + QUAD]
                    done = halve(dst.rearrange("p j g -> p g j"),
                                 dots_ps[(QUADS - 1) % 2][lane * FIELDS:(lane + 1) * FIELDS, :, 0, at:at + COLS])
            return done

        @block.tensor
        def _(pe):
            def transposes(k, t, first=False, between=None):
                for g in range(PAIR):
                    if g and between:
                        between()
                    pe.wait_ge(gathered[PAIR * k + g], 16 * t + 16)
                    if g == 0 and not (first and k < 2):
                        pe.wait_ge(rest_set, PAIRS * t + (k - 1))
                    for h in range(HALVES):
                        done = nc.tensor.transpose(turned_ps[k % 2][:, g, h, :],
                                                   emb[:, PAIR * k + g, h * P:(h + 1) * P], ident[:, :])
                done.then_inc(transposed, 1)

            def dots(k, t, first_block=False):
                q, first = divmod(PAIR * k, QUAD)
                pe.wait_ge(rest_set, PAIRS * t + (k + 1))
                if first == 0 and not (first_block and q < 2):
                    pe.wait_ge(z_set, QUADS * t + (q - 1))
                for g in range(PAIR):
                    for h in range(HALVES):
                        parts_of_x = split[:, k % SPLIT_BUFS, g, h, :, :]
                        done = nc.tensor.matmul(dots_ps[q % 2][:, first + g, :, :], parts_of_x[:, 0, :],
                                                parts_of_x, start=(h == 0), stop=(h == HALVES - 1))
                done.then_inc(dotted, 1)

            def whole_dots(groups):
                for g in groups:
                    for h in range(HALVES):
                        x = whole[:, g, h, :]
                        done = nc.tensor.matmul(dots_ps[(QUADS - 1) % 2][:, g, 0, :], x, x,
                                                start=(h == 0), stop=(h == HALVES - 1))
                return done

            def octet_parts(q, i, t, first=False, elsewhere=False):
                if i == 0:
                    pe.wait_ge(z_set, QUADS * t + (QUADS // OCTETS) * (q + 1))
                    pe.wait_ge(context_set, t + 1)
                if not (first and q == 0):
                    pe.wait_ge(parts_set[i], OCTETS * t + q)
                    if not elsewhere:
                        pe.wait_ge(h1_set[i], OCTETS * t + q)
                if q == 0 and not first:
                    pe.wait_ge((h2_dve, h2_act)[i], t)
                if q == 1 and i == 1 and not first:
                    pe.wait_ge(y_copied, t)
                for jj in range(COLS // PARTS):
                    for c in range(PARTS):
                        j = c * (COLS // PARTS) + jj
                        done = nc.tensor.matmul(parts_ps[i][c * PART:(c + 1) * PART, :],
                                                z[:, j, q * PART:(q + 1) * PART],
                                                w1_sb[:, j, i * NARROW:(i + 1) * NARROW],
                                                start=(jj == 0), stop=(jj == COLS // PARTS - 1))
                    for c in range(PARTS if jj == 0 else 0):
                        units = NARROW // PARTS
                        nc.tensor.matmul(parts_ps[i][c * PART:(c + 1) * PART, c * units:(c + 1) * units],
                                         context_now[:, q * PART:(q + 1) * PART],
                                         w1c_sb[:, i * NARROW + c * units:i * NARROW + (c + 1) * units],
                                         start=False, stop=False, skip_group_check=True)
                done.then_inc(parts_done, 1)

            def octet_fold(q, i, t, to=folded_ps):
                pe.wait_ge(parts_set[i], OCTETS * t + (q + 1))
                for n in range(i * N1 // 2, (i + 1) * N1 // 2):
                    done = nc.tensor.matmul(to[n], parts[i][:, q % 2, n % 2 * P:(n % 2 + 1) * P], fold[:, :],
                                            start=True, stop=True)
                done.then_inc(folded[i], 1)

            def second_layer(of):
                pe.wait_ge(h1_set[0], OCTETS * of + OCTETS)
                for m in range(N2):
                    for n in range(N1):
                        if m == 0 and n == N1 // 2:
                            pe.wait_ge(h1_set[1], OCTETS * of + OCTETS)
                        done = nc.tensor.matmul(h2_ps[m], w2_sb[:, n, m * P:(m + 1) * P], h1[:, n, :],
                                                start=(n == 0), stop=(n == N1 - 1))
                    done.then_inc(h2_done, 1)

            def late_second_layer(of):
                pe.wait_ge(h1_set[0], OCTETS * of + OCTETS)
                for n in range(N1):
                    if n == N1 // 2:
                        pe.wait_ge(h1_set[1], OCTETS * of + OCTETS)
                    for m in range(N2):
                        done = nc.tensor.matmul(late_h2_ps[m], w2_sb[:, n, m * P:(m + 1) * P], h1[:, n, :],
                                                start=(n == 0), stop=(n == N1 - 1))
                        if n == N1 - 1:
                            done.then_inc(h2_done, 1)

            def output(of, to=y_ps):
                pe.wait_ge(h2_dve, of + 1)
                if to is y_ps:
                    pe.wait_ge(h2_act, of + 1)
                for m in range(N2):
                    if m == 1 and to is not y_ps:
                        pe.wait_ge(h2_act, of + 1)
                    done = nc.tensor.matmul(to, w3_sb[:, m:m + 1], h2[:, m, :],
                                            start=(m == 0), stop=(m == N2 - 1))
                done.then_inc(y_done, 1)

            def block_of(t, steps=PAIRS, first=False, last=False):
                for k in range(steps):
                    before_layers, *after_layers = dots_due(k, last)

                    def dots_before():
                        if before_layers >= 0:
                            dots(before_layers, t, first)
                        elif not first:
                            dots(before_layers + PAIRS, t - 1)

                    transposes(k, t, first, dots_before)
                    if first and k == FIRST_PARTS:
                        pe.wait_ge(fold_set, 1)
                        pe.wait_ge(w1_in, 16 * W1_LOADS)
                        pe.wait_ge(w1c_in, 16)
                    for q, back in due(k, 0, first, last):
                        octet_parts(q, 0, t - back, first)
                    for q, back in due(k, 1, first, last):
                        octet_parts(q, 1, t - back, first)
                        octet_fold(q, 0, t - back)
                    for q, back in due(k, 2, first, last):
                        octet_fold(q, 1, t - back)
                    if k == LAYER2 and not first:
                        second_layer(t - 1)
                    if k == OUTPUT and not first:
                        pe.wait_ge(h1_set[1], OCTETS * t + 1)
                        output(t - 1)
                    for pair in after_layers:
                        dots(pair, t)

            def whole_transposes(g, bank):
                for h in range(HALVES):
                    done = nc.tensor.transpose(turned_ps[bank][:, g % PAIR, h, :],
                                               emb[:, GROUPS - QUAD + g, h * P:(h + 1) * P], ident[:, :])
                done.then_inc(transposed, 1)

            pe.wait_ge(ident_set, 1)
            block_of(0, first=True)
            pe.wait_ge(w2_in, 16)
            pe.wait_ge(w3_in, 16)
            with pe.Fori(1, BLOCKS - 1) as t:
                block_of(t)
            t = BLOCKS - 1
            block_of(t, PAIRS - 3, last=True)
            transposes(PAIRS - 3, t, between=lambda: dots(PAIRS - 4, t))
            octet_fold(1, 1, t)
            transposes(PAIRS - 2, t)
            octet_parts(2, 0, t)
            dots(PAIRS - 3, t)
            pe.wait_ge(gathered[GROUPS - 2], 16 * BLOCKS)
            pe.wait_ge(rest_set, PAIRS * t + (PAIRS - 2))
            whole_transposes(2, 1)
            pe.wait_ge(whole_set, 1)
            pe.wait_ge(z_set, QUADS * BLOCKS - 2)
            whole_dots((0, 1)).then_inc(dotted, 1)
            pe.wait_ge(gathered[GROUPS - 1], 16 * BLOCKS)
            whole_transposes(3, 0)
            pe.wait_ge(whole_set, 2)
            whole_dots((2,))
            octet_fold(2, 0, t)
            pe.wait_ge(whole_set, 3)
            whole_dots((3,)).then_inc(dotted, 1)
            octet_parts(2, 1, t)
            pe.wait_ge(z_act, 1)
            octet_parts(3, 0, t)
            octet_parts(3, 1, t, elsewhere=True)
            octet_fold(3, 0, t)
            octet_fold(2, 1, t, late_folded_ps)
            octet_fold(3, 1, t)
            late_second_layer(t)
            output(t, late_y_ps)

        @block.vector
        def _(dve):
            def columns(at):
                return slice(at, at + REFILL) if isinstance(at, int) else bass.ds(at, REFILL)

            def refill(half, at):
                nc.vector.tensor_scalar(rows_now[half][:, :], ids_sb[:, at], ids_sb[:, 0:1], None,
                                        ALU.add).then_inc(refilled[half], 1)

            def spread(q, t, lanes, first=False):
                octet, place = divmod(q * QUAD, OCTET)
                if 0 in lanes:
                    dve.wait_ge(halved_set, QUADS * t + (q + 1))
                    if place == 0 and not first:
                        dve.wait_ge(parts_done, 2 * OCTETS * t + (2 * (octet + 1) - 2 * OCTETS))
                for lane in lanes:
                    at_z = octet * PART + lane * OCTET + place
                    for c in range(P // FIELDS):
                        at = lane * FIELDS + c * COLS
                        of_lane = slice(lane * FIELDS, (lane + 1) * FIELDS)
                        dst = z[c * FIELDS:(c + 1) * FIELDS, :, at_z:at_z + QUAD]
                        done = nc.vector.tensor_tensor(dst.rearrange("p j g -> p g j"),
                                                       dots_ps[q % 2][of_lane, :, 1, at:at + COLS],
                                                       halved[of_lane, q % 2, :, c * COLS:(c + 1) * COLS], ALU.add)
                if LANES - 1 in lanes:
                    done.then_inc(z_set, 1)

            def relu(dst, src, bias):
                return nc.vector.tensor_scalar(dst, src, bias, 0.0, ALU.add, ALU.max)

            def copy_parts(q, t):
                dve.wait_ge(parts_done, 2 * OCTETS * t + (2 * q + 1))
                nc.vector.tensor_copy(parts[0][:, q % 2, :], parts_ps[0]).then_inc(parts_set[0], 1)

            def relu_folded(q, t):
                dve.wait_ge(folded[0], OCTETS * t + (q + 1))
                for n in range(N1 // 2):
                    done = relu(h1[:, n, q * PART:(q + 1) * PART], folded_ps[n], b1_sb[:, n:n + 1])
                done.then_inc(h1_set[0], 1)

            def relu_second(t, src=h2_ps):
                dve.wait_ge(h2_done, N2 * t + 1)
                relu(h2[:, 0, :], src[0], b2_sb[:, 0:1]).then_inc(h2_dve, 1)

            def copy_y(t, src=y_ps):
                dve.wait_ge(y_done, t + 1)
                nc.vector.tensor_copy(y[:, samples(t)], src).then_inc(y_copied, 1)

            def set_context(t, first):
                if first:
                    dve.wait_ge(context_in, 16)
                else:
                    dve.wait_ge(parts_done, 2 * OCTETS * t)
                nc.vector.tensor_copy(context_now[:, :], context_sb[:, samples(t)]).then_inc(context_set, 1)

            def layers_step(k, t, first, last):
                for q, back in due(k, 1, first, last):
                    copy_parts(q, t - back)
                if k == LAYER2 + 1 and not first:
                    relu_second(t - 1)
                if k == OUTPUT + 1 and not first:
                    copy_y(t - 1)

            def block_of(t, steps=PAIRS, first=False, last=False):
                for k in range(steps):
                    if k == PAIRS // 2 + 1 and not last:
                        refill(0, columns(t * GROUPS + (1 + GROUPS)))
                    layers_step(k, t, first, last)
                    if k == LAYER2:
                        set_context(t, first)
                    dve.wait_ge(rounded, PAIRS * t + (k + 1))
                    parts_of_x = split[:, k % SPLIT_BUFS, :, :, :, :]
                    nc.vector.tensor_tensor(parts_of_x[:, :, :, 1, :], turned_ps[k % 2][:, :, :, :],
                                            parts_of_x[:, :, :, 0, :].bitcast(fp32),
                                            ALU.subtract).then_inc(rest_set, 1)
                    if k == PAIRS - 1 and not last:
                        refill(1, columns(t * GROUPS + (1 + GROUPS + REFILL)))
                    q, lanes = spread_due(k, last)
                    if q is not None and q >= 0:
                        spread(q, t, lanes, first)
                    elif q is not None and not first:
                        spread(q + QUADS, t - 1, lanes)

            dve.wait_ge(ids_in, 16)
            refill(0, columns(1))
            refill(1, columns(1 + REFILL))
            dve.wait_ge(ident_set, 1)
            nc.vector.tensor_reduce(fold[:, :], ident[:, :].rearrange("p (c s) -> p s c", c=PARTS),
                                    mybir.AxisListType.X, ALU.add).then_inc(fold_set, 1)
            dve.wait_ge(b1_in, 16)
            dve.wait_ge(b2_in, 16)
            block_of(0, first=True)
            with dve.Fori(1, BLOCKS - 1) as t:
                block_of(t)
            t = BLOCKS - 1
            block_of(t, PAIRS - 2, last=True)
            copy_parts(2, t)
            spread(QUADS - 2, t, range(LANES))
            relu_folded(2, t)
            dve.wait_ge(dotted, PAIRS * BLOCKS)
            spread_whole(lambda dst, src: nc.vector.tensor_scalar(dst, src, 0.5, None, ALU.mult),
                         range(LANES // 2)).then_inc(z_set, 1)
            copy_parts(3, t)
            relu_folded(3, t)
            relu_second(t, late_h2_ps)
            copy_y(t, late_y_ps)

        @block.scalar
        def _(act):
            def relu(dst, src, bias):
                return nc.scalar.activation(dst, src, ACT.Relu, bias=bias)

            def copy_parts(q, t):
                act.wait_ge(parts_done, 2 * OCTETS * t + (2 * q + 2))
                nc.scalar.copy(parts[1][:, q % 2, :], parts_ps[1]).then_inc(parts_set[1], 1)

            def relu_folded(q, i, t, first=False, src=folded_ps):
                act.wait_ge(folded[i], OCTETS * t + (q + 1))
                if q == 0 and i == 0 and not first:
                    act.wait_ge(h2_done, N2 * t)
                for n in range(i * N1 // 2, (i + 1) * N1 // 2):
                    done = relu(h1[:, n, q * PART:(q + 1) * PART], src[n], b1_sb[:, n:n + 1])
                done.then_inc(h1_set[i], 1)

            def relu_second(t, src=h2_ps):
                act.wait_ge(h2_done, N2 * t + 2)
                relu(h2[:, 1, :], src[1], b2_sb[:, 1:2]).then_inc(h2_act, 1)

            def layers_step(k, t, first, last):
                for q, back in due(k, 2, first, last):
                    copy_parts(q, t - back)
                    relu_folded(q, 0, t - back, first)
                for q, back in due(k, 3, first, last):
                    relu_folded(q, 1, t - back, first)
                if k == LAYER2 + 1 and not first:
                    relu_second(t - 1)

            def halve(q, t, first=False):
                act.wait_ge(dotted, PAIRS * t + PER_QUAD * (q + 1))
                if not (first and q < 2):
                    act.wait_ge(z_set, QUADS * t + (q - 1))
                for lane in range(LANES):
                    of_lane = slice(lane * FIELDS, (lane + 1) * FIELDS)
                    done = nc.scalar.activation(halved[of_lane, q % 2, :, :], dots_ps[q % 2][of_lane, :, 0, of_lane],
                                                ACT.Copy, scale=0.5)
                done.then_inc(halved_set, 1)

            def block_of(t, steps=PAIRS, first=False, last=False):
                for k in range(steps):
                    layers_step(k, t, first, last)
                    act.wait_ge(transposed, PAIRS * t + (k + 1))
                    if not (first and k < SPLIT_BUFS):
                        act.wait_ge(dotted, PAIRS * t + (k - SPLIT_BUFS + 1))
                    nc.scalar.copy(split[:, k % SPLIT_BUFS, :, :, 0, :], turned_ps[k % 2][:, :, :, :])\
                        .then_inc(rounded, 1)
                    q, lanes = spread_due(k, last)
                    if q is not None and 0 in lanes:
                        if q >= 0:
                            halve(q, t, first)
                        elif not first:
                            halve(q + QUADS, t - 1)

            def copy_whole(groups, bank, count):
                act.wait_ge(transposed, count)
                at = groups[0] % PAIR
                nc.scalar.copy(whole[:, groups[0]:groups[0] + len(groups), :, :],
                               turned_ps[bank][:, at:at + len(groups), :, :]).then_inc(whole_set, 1)

            act.wait_ge(b1_in, 16)
            act.wait_ge(b2_in, 16)
            block_of(0, first=True)
            with act.Fori(1, BLOCKS - 1) as t:
                block_of(t)
            t = BLOCKS - 1
            block_of(t, PAIRS - 2, last=True)
            relu_folded(1, 1, t)
            copy_whole((0, 1), 0, PAIRS * BLOCKS - 1)
            halve(QUADS - 2, t)
            copy_whole((2,), 1, PAIRS * BLOCKS)
            copy_whole((3,), 0, PAIRS * BLOCKS + 1)
            act.wait_ge(dotted, PAIRS * BLOCKS)
            spread_whole(lambda dst, src: nc.scalar.activation(dst, src, ACT.Copy, scale=0.5),
                         range(LANES // 2, LANES)).then_inc(z_act, 1)
            copy_parts(2, t)
            copy_parts(3, t)
            relu_folded(2, 1, t, src=late_folded_ps)
            relu_folded(3, 1, t)
            relu_second(t, late_h2_ps)


def _pair_rows():
    import numpy as np
    at = -np.ones((P, COLS), np.int64)
    i, j = np.triu_indices(FIELDS, k=1)
    at[(j // COLS) * FIELDS + i, j % COLS] = np.arange(len(i))
    at[(i // COLS) * FIELDS + j, i % COLS] = np.arange(len(i))
    return at


def kernel(**inputs):
    import numpy as np
    import concourse.bacc as bacc
    from concourse.bass_utils import run_bass_kernel_spmd

    tables = [np.asarray(inputs[f"tbl_{f}"]) for f in range(FIELDS)]
    first_row = np.concatenate([[0], np.cumsum([t.shape[0] for t in tables])[:-1]]).astype(np.int32)
    ids = np.asarray(inputs["ids"]).reshape(BLOCKS, OCTETS, LANES, OCTET, FIELDS)
    w1 = np.asarray(inputs["W_top1"])
    at = _pair_rows()
    w1_planes = np.zeros((P, COLS, HIDDEN1), w1.dtype)
    w1_planes[at >= 0] = w1[at[at >= 0]]
    arrays = {
        "ids": np.concatenate([np.tile(first_row, LANES).reshape(P, 1),
                               ids.transpose(2, 4, 0, 1, 3).reshape(P, BLOCKS * GROUPS)], axis=1),
        "tables": np.concatenate(tables, axis=0),
        "context_t": np.ascontiguousarray(np.asarray(inputs["dense_ctx"]).T),
        "w1": w1_planes,
        "w1c": np.ascontiguousarray(w1[-CONTEXT:]),
        "b1": np.ascontiguousarray(np.asarray(inputs["b_top1"]).reshape(N1, P).T),
        "w2": np.asarray(inputs["W_top2"]),
        "b2": np.ascontiguousarray(np.asarray(inputs["b_top2"]).reshape(N2, P).T),
        "w3": np.ascontiguousarray(np.asarray(inputs["W_top3"]).reshape(N2, P).T),
    }
    nc = bacc.Bacc("TRN2", target_bir_lowering=False, num_devices=1)
    args = [nc.dram_tensor(name, a.shape, mybir.dt.from_np(a.dtype), kind="ExternalInput").ap()
            for name, a in arrays.items()]
    out = nc.dram_tensor("y_out", (1, BATCH), mybir.dt.float32, kind="ExternalOutput").ap()
    dlrm_tower(nc, *args, out)
    r = run_bass_kernel_spmd(nc, [arrays], core_ids=[0])
    return r.results[0]["y_out"].reshape(BATCH, 1)
```
